# Optimizing a Trainium2 kernel written in Bass

```python
import numpy as np
import jax
import jax.numpy as jnp

def _softmax(x, axis=-1):
    return jax.nn.softmax(x, axis=axis)

def _gelu(x):
    return jax.nn.gelu(x, approximate=True)

def _silu(x):
    return jax.nn.silu(x)

def _sigmoid(x):
    return jax.nn.sigmoid(x)

def _layernorm(x, axis=-1, eps=1e-05):
    m = jnp.mean(x, axis=axis, keepdims=True)
    v = jnp.var(x, axis=axis, keepdims=True)
    return (x - m) / jnp.sqrt(v + eps)

def _scatter_add(tgt, idx, src, axis=0):
    return tgt.at[idx].add(src)

def _segment_sum(src, seg, n):
    return jax.ops.segment_sum(src, seg, n)
kernel_name = 'mk_sandwich_d1_jaxref_r8_bac0d4'

def setup_inputs(seed: int=0):
    np.random.seed(seed)
    _w = jnp.asarray

    def _L0_attn_setup():
        import jax, jax.numpy as jnp
        import numpy as np
        import math
        B, L, D, H = (2, 256, 128, 16)

        def _log_sparse_mask(L):
            m = np.zeros((L, L), dtype=bool)
            for i in range(L):
                for k in range(int(math.log2(i + 1)) + 1):
                    j = i - 2 ** k
                    if j >= 0:
                        m[i, j] = True
                m[i, i] = True
            return m
        key = jax.random.key(seed)
        ks = jax.random.split(key, 9)
        s = 0.02
        return {'x': jax.random.normal(ks[0], (B, L, D), dtype=jnp.float32), 'Wq': jax.random.normal(ks[1], (D, D), dtype=jnp.float32) * s, 'bq': jnp.zeros((D,), dtype=jnp.float32), 'Wk': jax.random.normal(ks[2], (D, D), dtype=jnp.float32) * s, 'bk': jnp.zeros((D,), dtype=jnp.float32), 'Wv': jax.random.normal(ks[3], (D, D), dtype=jnp.float32) * s, 'bv': jnp.zeros((D,), dtype=jnp.float32), 'Wo': jax.random.normal(ks[4], (D, D), dtype=jnp.float32) * s, 'bo': jnp.zeros((D,), dtype=jnp.float32)}
    _L0_attn_in = _L0_attn_setup()

    def _L0_ffn_setup():
        import jax, jax.numpy as jnp
        import numpy as np
        import math
        BETA = 0.9
        THRESHOLD = 1.0
        NUM_STEPS = 5
        ALPHA = 2.0

        @jax.custom_vjp
        def spike_fn(u):
            return (u > 0).astype(u.dtype)

        def _spike_fwd(u):
            return (spike_fn(u), u)

        def _spike_bwd(u, g):
            s = jnp.pi / 2.0 * ALPHA * u
            return (g * (ALPHA / 2.0) / (1.0 + s * s),)
        spike_fn.defvjp(_spike_fwd, _spike_bwd)
        key = jax.random.key(seed)
        k1, k2, k3 = jax.random.split(key, 3)
        n_embd = 128
        x = jax.random.normal(k1, (4, 256, n_embd), dtype=jnp.float32)
        W_fc = jax.random.normal(k2, (4 * n_embd, n_embd), dtype=jnp.float32) / math.sqrt(n_embd)
        W_proj = jax.random.normal(k3, (n_embd, 4 * n_embd), dtype=jnp.float32) / math.sqrt(4 * n_embd)
        return {'x': x, 'W_fc': W_fc, 'W_proj': W_proj}
    _L0_ffn_in = _L0_ffn_setup()
    _d = {'L0_attn_x': _L0_attn_in['x'], 'L0_attn_Wq': _L0_attn_in['Wq'], 'L0_attn_bq': _L0_attn_in['bq'], 'L0_attn_Wk': _L0_attn_in['Wk'], 'L0_attn_bk': _L0_attn_in['bk'], 'L0_attn_Wv': _L0_attn_in['Wv'], 'L0_attn_bv': _L0_attn_in['bv'], 'L0_attn_Wo': _L0_attn_in['Wo'], 'L0_attn_bo': _L0_attn_in['bo'], 'L0_ffn_W_fc': _L0_ffn_in['W_fc'], 'L0_ffn_W_proj': _L0_ffn_in['W_proj']}
    _x0 = _d['L0_attn_x']
    _d['L0_attn_x'] = jax.random.normal(jax.random.fold_in(jax.random.key(seed), 1), (4, 1024, 128), dtype=_x0.dtype)
    del _x0
    return _d

def reference(L0_attn_x, L0_attn_Wq, L0_attn_bq, L0_attn_Wk, L0_attn_bk, L0_attn_Wv, L0_attn_bv, L0_attn_Wo, L0_attn_bo, L0_ffn_W_fc, L0_ffn_W_proj):

    def _L0_attn_ref(x, Wq, bq, Wk, bk, Wv, bv, Wo, bo):
        import jax, jax.numpy as jnp
        import numpy as np
        import math
        B, L, D, H = (2, 256, 128, 16)

        def _log_sparse_mask(L):
            m = np.zeros((L, L), dtype=bool)
            for i in range(L):
                for k in range(int(math.log2(i + 1)) + 1):
                    j = i - 2 ** k
                    if j >= 0:
                        m[i, j] = True
                m[i, i] = True
            return m
        Bx, Lx, Dx = x.shape
        dh = Dx // H
        scale = math.sqrt(dh)
        mask = jnp.asarray(_log_sparse_mask(Lx))
        q = (x @ Wq.T + bq).reshape(Bx, Lx, H, dh)
        k = (x @ Wk.T + bk).reshape(Bx, Lx, H, dh)
        v = (x @ Wv.T + bv).reshape(Bx, Lx, H, dh)
        raw = jnp.einsum('blhd,bmhd->bhlm', q, k)
        scores = jnp.where(mask, raw, 0.0) / scale
        attn = jax.nn.softmax(scores, axis=-1)
        out = jnp.einsum('bhlm,bmhd->blhd', attn, v).reshape(Bx, Lx, Dx)
        return out @ Wo.T + bo

    def _L0_ffn_ref(x, W_fc, W_proj):
        import jax, jax.numpy as jnp
        import numpy as np
        import math
        BETA = 0.9
        THRESHOLD = 1.0
        NUM_STEPS = 5
        ALPHA = 2.0

        @jax.custom_vjp
        def spike_fn(u):
            return (u > 0).astype(u.dtype)

        def _spike_fwd(u):
            return (spike_fn(u), u)

        def _spike_bwd(u, g):
            s = jnp.pi / 2.0 * ALPHA * u
            return (g * (ALPHA / 2.0) / (1.0 + s * s),)
        spike_fn.defvjp(_spike_fwd, _spike_bwd)
        h = jnp.square(jax.nn.relu(jnp.einsum('bsd,fd->bsf', x, W_fc)))
        y = jnp.einsum('bsf,df->bsd', h, W_proj)

        def step(mem, _):
            reset = jax.lax.stop_gradient(spike_fn(mem - THRESHOLD))
            mem_new = BETA * mem + y - reset * THRESHOLD
            spk = spike_fn(mem_new - THRESHOLD)
            return (mem_new, spk)
        mem0 = jnp.zeros_like(y)
        _, spks = jax.lax.scan(step, mem0, None, length=NUM_STEPS)
        return jnp.sum(spks, axis=0) / NUM_STEPS
    x = L0_attn_x
    x = x + _layernorm(_L0_attn_ref(_layernorm(x, axis=-1), L0_attn_Wq, L0_attn_bq, L0_attn_Wk, L0_attn_bk, L0_attn_Wv, L0_attn_bv, L0_attn_Wo, L0_attn_bo), axis=-1)
    x = x + _layernorm(_L0_ffn_ref(_layernorm(x, axis=-1), L0_ffn_W_fc, L0_ffn_W_proj), axis=-1)
    return x

_drawn_inputs = setup_inputs


def setup_inputs(seed=0):
    import zlib

    import numpy as np

    out = dict(_drawn_inputs(seed))
    spreads = {'L0_attn_bq': (0.0, 0.8),
     'L0_attn_bk': (0.0, 0.8),
     'L0_attn_bv': (0.0, 0.1),
     'L0_attn_bo': (0.0, 0.1)}
    factors = {'L0_attn_Wq': 8.0, 'L0_attn_Wk': 8.0}
    for name, (base, spread) in spreads.items():
        noise = np.random.default_rng([zlib.crc32(name.encode()), seed]).standard_normal(out[name].shape)
        drawn = base * np.exp(spread * noise) if base else spread * noise
        out[name] = jnp.asarray(drawn.astype(out[name].dtype))
    for name, factor in factors.items():
        out[name] = (out[name] * factor).astype(out[name].dtype)
    return out
```

```python
from contextlib import ExitStack

import numpy as np


import concourse.bass as bass
from concourse import mybir

F32 = mybir.dt.float32
F32R = mybir.dt.float32r
ALU = mybir.AluOpType
ACT = mybir.ActivationFunctionType
AX = mybir.AxisListType

BETA, THRESHOLD, STEPS = 0.9, 1.0, 5
EPS = 1e-5
P = 128


def spikes_of(y):
    y = np.float32(y)
    mem, spikes = np.float32(0), 0
    for _ in range(STEPS):
        reset = np.float32(mem - np.float32(THRESHOLD) > 0)
        mem = np.float32(np.float32(np.float32(BETA) * mem) + y) - reset * np.float32(THRESHOLD)
        spikes += int(mem - np.float32(THRESHOLD) > 0)
    return spikes


def spike_thresholds():
    found = []
    for n in range(STEPS):
        low, high = np.float32(0), np.float32(2 * THRESHOLD)
        while np.nextafter(low, high) < high:
            middle = np.float32((low + high) / 2)
            if middle in (low, high):
                middle = np.nextafter(low, high)
            low, high = (middle, high) if spikes_of(middle) <= n else (low, middle)
        found.append(float(low))
    return found


def log_sparse_block(nc, x, wq_t, bq, wk_t, bk, wv_t, bv, wo_t, bo, wfc_t, wproj_t, out):
    B, L, D = x.shape
    H = 16
    HD = D // H
    FF = wfc_t.shape[1]
    FB = FF // P
    TB = L // P
    HALF = L // 2
    OFFSETS = [0] + [1 << k for k in range(L.bit_length() - 1)]
    NK = len(OFFSETS)
    SLOTS = NK + 1
    BASE = NK
    PAD = OFFSETS[-1]
    SCALE = 1.0 / float(np.sqrt(HD))
    GROUPS = [range(g, min(g + 4, NK)) for g in range(0, NK, 4)]
    PAIRS = [(k, k + 1) for k in range(0, NK - 1, 2)]
    QT = 2 * P
    NQ = L // QT
    THRESHOLDS = spike_thresholds()
    SPREADS = [(pair, 2 * c, 2) for pair in PAIRS for c in range(NQ)]
    SPREADS += [((NK - 1,), PAD // P + 2 * c, 2) for c in range((L - PAD) // QT)]
    SPREADS += [((BASE,), 4 * c, 4) for c in range(TB // 4)]
    NW = 3
    NX = 2
    NS = len(SPREADS)
    assert D == P and L == 1024 and NS % NW == 0 and SLOTS * P == 3 * 512

    x_rows = x.rearrange("b (i p) d -> b p i d", p=P)
    out_rows = out.rearrange("b (i p) d -> b p i d", p=P)

    ctx = ExitStack()
    with ctx:
        def sb(name, shape, dt=F32):
            return ctx.enter_context(nc.sbuf_tensor(name, shape, dt))

        def pb(name, shape, dt=F32):
            return ctx.enter_context(nc.psum_tensor(name, shape, dt))

        def sem(name):
            return ctx.enter_context(nc.semaphore(name))

        wq_sb, wk_sb, wv_sb, wo_sb = (sb(n, [P, D]) for n in ("wq_sb", "wk_sb", "wv_sb", "wo_sb"))
        wfc_sb = sb("wfc_sb", [P, FF])
        wproj_sb = sb("wproj_sb", [P, FB, D])
        bias_cols = sb("bias_cols", [P, 3])
        bo_row = sb("bo_row", [P, D])
        bo_hi, bo_lo = sb("bo_hi", [P, D], F32R), sb("bo_lo", [P, D], F32R)
        first_row = sb("first_row", [P, P])
        first_row_r = sb("first_row_r", [P, P], F32R)
        ident = sb("ident", [P, P])
        head_sum = sb("head_sum", [P, 2, 32])
        spread = sb("spread", [P, TB, P])
        spread_r = sb("spread_r", [P, TB, P], F32R)
        neg_half = sb("neg_half", [P, TB])
        x_all = sb("x_all", [P, B, TB, D])
        xn_in, xn_ff = sb("xn_in", [P, TB, D]), sb("xn_ff", [P, TB, D])
        xnT_in, xnT_ff = sb("xnT_in", [P, L]), sb("xnT_ff", [P, L])
        qT, kT = sb("qT", [P, L]), sb("kT", [P, L])
        vT = sb("vT", [P, PAD + L])
        v_parts = sb("v_parts", [P, 2])
        v_total = sb("v_total", [P, 1])
        qk = sb("qk", [P, NK, L])
        wv = sb("wv", [P, NK, L])
        s_max, s_sum, z_inv = sb("s_max", [P, P]), sb("s_sum", [P, P]), sb("z_inv", [P, P])
        es = sb("es", [P, SLOTS, P])
        wt = sb("wt", [P, SLOTS, P])
        wt_hi, wt_lo = sb("wt_hi", [P, SLOTS, P], F32R), sb("wt_lo", [P, SLOTS, P], F32R)
        attn = sb("attn", [P, TB, D])
        hid = sb("hid", [P, FB, L])
        y_sb = sb("y_sb", [P, TB, D])
        spikes = sb("spikes", [P, TB, D])
        LN = ("in", "mid", "ff", "out")
        sums = {n: sb(f"sums_{n}", [P, TB, 6]) for n in LN}
        mom = {n: sb(f"mom_{n}", [P, TB, 2]) for n in LN}
        neg_mean = {n: sb(f"neg_mean_{n}", [P, TB]) for n in LN}
        var_eps = {n: sb(f"var_eps_{n}", [P, TB]) for n in LN}
        rstd = {n: sb(f"rstd_{n}", [P, TB]) for n in LN}
        shift = {n: sb(f"shift_{n}", [P, TB]) for n in LN}
        scores = pb("scores", [P, SLOTS, P])
        wbank = [pb(f"wbank{i}", [P, 512]) for i in range(NW)]
        xbank = [pb(f"xbank{i}", [P, 512]) for i in range(NX)]

        NG = len(GROUPS)
        MERGES = [(0, 2, 2 * NQ), (4, 6, 4 * NQ), (0, 4, 4 * NQ), (0, 8, 5 * NQ)]
        NM = len(MERGES)
        NLOADS = 9

        def first(b):
            return isinstance(b, int) and b == 0

        def per_slot(row):
            return row.unsqueeze(1).to_broadcast([P, NK, P])

        def bank_rows(h):
            return xbank[h][:, :].rearrange("p (i d) -> p i d", d=D)

        def two_offsets(tokens, step):
            partitions, run = tokens.ap
            return bass.AP(tensor=tokens.tensor, offset=tokens.offset,
                           ap=[list(partitions), [step, 2], list(run)])

        weights_in, bo_in, x_in, stored = sem("weights_in"), sem("bo_in"), sem("x_in"), sem("stored")
        pool_set, dve_set = sem("pool_set"), sem("dve_set")
        ln_sums = {n: sem(f"ln_sums_{n}") for n in LN}
        ln_mom = {n: sem(f"ln_mom_{n}") for n in LN}
        ln_var = {n: sem(f"ln_var_{n}") for n in LN}
        ln_rstd = {n: sem(f"ln_rstd_{n}") for n in LN}
        ln_shift = {n: sem(f"ln_shift_{n}") for n in LN}
        ln_done = {n: sem(f"ln_done_{n}") for n in LN}
        turned = {n: sem(f"turned_{n}") for n in ("in", "ff")}
        xnT_ready = {n: sem(f"xnT_ready_{n}") for n in ("in", "ff")}
        qk_filled, qk_loaded = sem("qk_filled"), sem("qk_loaded")
        v_filled, v_loaded = sem("v_filled"), sem("v_loaded")
        attn_filled, attn_ready = sem("attn_filled"), sem("attn_ready")
        fc_filled, relu_ready = sem("fc_filled"), sem("relu_ready")
        y_filled, y_ready = sem("y_filled"), sem("y_ready")
        hid_ready = sem("hid_ready")
        v_summed = sem("v_summed")
        qk_ready = sem("qk_ready")
        scores_ready = sem("scores_ready")
        max_ready, shifted, exp_ready = sem("max_ready"), sem("shifted"), sem("exp_ready")
        sum_ready, z_ready, inv_ready = sem("sum_ready"), sem("z_ready"), sem("inv_ready")
        diff_ready, wt_ready = sem("diff_ready"), sem("wt_ready")
        hi_ready, lo_ready = sem("hi_ready"), sem("lo_ready")
        spread_ready = sem("spread_ready")
        wv_ready = sem("wv_ready")
        merged = sem("merged")
        x1_ready, spike_step, out_ready = sem("x1_ready"), sem("spike_step"), sem("out_ready")

        block = ctx.enter_context(nc.Block())

        @block.sync
        def _(sp):
            def load_x(b):
                sp.dma_start(x_all[:, b, :, :], x_rows[b, :, :, :]).then_inc(x_in, 16)

            load_x(0)
            loads = [(wq_sb[:, :], wq_t), (wk_sb[:, :], wk_t), (bias_cols[:, 0:1], bq),
                     (bias_cols[:, 1:2], bk), (bias_cols[:, 2:3], bv), (wv_sb[:, :], wv_t),
                     (wo_sb[:, :], wo_t), (wfc_sb[:, :], wfc_t),
                     (wproj_sb[:, :, :], wproj_t.rearrange("(f p) d -> p f d", p=P))]
            assert len(loads) == NLOADS
            for dst, src in loads:
                sp.dma_start(dst, src).then_inc(weights_in, 16)
            sp.wait_ge(pool_set, 1)
            sp.dma_start(bo_row[0:1, :], bo).then_inc(bo_in, 16)
            for b in range(1, B):
                sp.wait_ge(x_in, 16 * b)
                load_x(b)
            for b in range(B):
                sp.wait_ge(out_ready, b + 1)
                sp.dma_start(out_rows[b, :, :, :], x_all[:, b, :, :]).then_inc(stored, 16)
            sp.wait_ge(stored, 16 * B)

        @block.gpsimd
        def _(pool):
            g = nc.gpsimd
            g.memset(bo_row[:, :], 0.0).then_inc(pool_set, 1)
            g.memset(ident[:, :], 0.0)
            g.memset(first_row[:, :], 0.0)
            g.memset(head_sum[:, :, :], 1.0)
            g.memset(spread[:, :, :], 0.0)
            g.memset(neg_half[:, :], -0.5).then_inc(pool_set, 1)
            pool.wait_ge(pool_set, 2)
            g.affine_select(out=ident[:, :], in_=ident[:, :], compare_op=ALU.not_equal, fill=1.0,
                            base=0, pattern=[[-1, P]], channel_multiplier=1)
            g.affine_select(out=first_row[:, :], in_=first_row[:, :], compare_op=ALU.not_equal,
                            fill=1.0, base=0, pattern=[[0, P]], channel_multiplier=1)
            g.affine_select(out=head_sum[:, :, :], in_=head_sum[:, :, :], compare_op=ALU.is_ge,
                            fill=0.0, base=0, pattern=[[HD * H, 2], [-HD, 2 * H]],
                            channel_multiplier=1).then_inc(pool_set, 1)
            pool.wait_ge(pool_set, 3)
            g.affine_select(out=head_sum[:, :, :], in_=head_sum[:, :, :], compare_op=ALU.is_ge,
                            fill=0.0, base=HD - 1, pattern=[[-HD * H, 2], [HD, 2 * H]],
                            channel_multiplier=-1)
            for t in range(TB):
                part = spread[:, t, :].rearrange("p (h d) -> p h d", d=HD)
                last = g.affine_select(out=part, in_=part, compare_op=ALU.not_equal, fill=1.0,
                                       base=-H * t, pattern=[[-1, H], [0, HD]], channel_multiplier=1)
            last.then_inc(pool_set, 1)

            def rsqrt(n, b):
                pool.wait_ge(ln_var[n], b + 1)
                if not first(b):
                    pool.wait_ge(ln_done[n], 2 * b)
                g.tensor_tensor(out=rstd[n][:, :], in0=var_eps[n][:, :], in1=neg_half[:, :],
                                op=ALU.pow).then_inc(ln_rstd[n], 1)
                pool.wait_ge(ln_rstd[n], b + 1)
                g.tensor_tensor(out=shift[n][:, :], in0=neg_mean[n][:, :], in1=rstd[n][:, :],
                                op=ALU.mult).then_inc(ln_shift[n], 1)

            def differences(b):
                pool.wait_ge(exp_ready, b + 1)
                if not first(b):
                    pool.wait_ge(lo_ready, b)
                g.tensor_tensor(out=wt[:, 0:NK, :], in0=es[:, 0:NK, :], in1=per_slot(es[:, BASE, :]),
                                op=ALU.subtract).then_inc(diff_ready, 1)

            def normalise(b):
                pool.wait_ge(inv_ready, b + 1)
                pool.wait_ge(diff_ready, b + 1)
                g.tensor_tensor(out=wt[:, BASE, :], in0=es[:, BASE, :], in1=z_inv[:, :], op=ALU.mult)
                g.tensor_tensor(out=wt[:, 0:NK, :], in0=wt[:, 0:NK, :], in1=per_slot(z_inv[:, :]),
                                op=ALU.mult).then_inc(wt_ready, 1)

            def low_parts(b):
                pool.wait_ge(hi_ready, b + 1)
                if not first(b):
                    pool.wait_ge(spread_ready, NS * b)
                g.tensor_tensor(out=wt_lo[:, :, :], in0=wt[:, :, :], in1=wt_hi[:, :, :].bitcast(F32),
                                op=ALU.subtract).then_inc(lo_ready, 1)

            def merge(b):
                for n, (into, other, spreads) in enumerate(MERGES):
                    pool.wait_ge(wv_ready, NS * b + spreads)
                    if n >= 2:
                        pool.wait_ge(merged, NM * b + n)
                    g.tensor_tensor(out=wv[:, into:into + 2, :], in0=wv[:, into:into + 2, :],
                                    in1=wv[:, other:other + 2, :], op=ALU.add).then_inc(merged, 1)

            def residual(b):
                pool.wait_ge(ln_done["mid"], 2 * b + 2)
                g.tensor_tensor(out=x_all[:, b, :, :], in0=x_all[:, b, :, :], in1=attn[:, :, :],
                                op=ALU.add).then_inc(x1_ready, 1)

            def final(b):
                pool.wait_ge(ln_done["out"], 2 * b + 2)
                g.tensor_tensor(out=x_all[:, b, :, :], in0=x_all[:, b, :, :], in1=spikes[:, :, :],
                                op=ALU.add).then_inc(out_ready, 1)

            def step(b, before, after):
                if before:
                    rsqrt("mid", b - 1)
                    residual(b - 1)
                    rsqrt("ff", b - 1)
                differences(b)
                normalise(b)
                low_parts(b)
                if after:
                    rsqrt("in", b + 1)
                merge(b)
                if before:
                    rsqrt("out", b - 1)
                    final(b - 1)

            rsqrt("in", 0)
            step(0, False, True)
            for b in range(1, B - 1):
                step(b, True, True)
            step(B - 1, True, False)
            rsqrt("mid", B - 1)
            residual(B - 1)
            rsqrt("ff", B - 1)
            rsqrt("out", B - 1)
            final(B - 1)

        @block.scalar
        def _(act):
            s = nc.scalar

            def norm(n, b, src, dst):
                act.wait_ge(ln_shift[n], b + 1)
                for i in range(TB):
                    row = s.activation(dst[:, i, :], src[:, i, :], ACT.Identity,
                                       bias=shift[n][:, i:i + 1], scale=rstd[n][:, i:i + 1])
                    if i % 4 == 3:
                        row.then_inc(ln_done[n], 1)

            def transposed(n, b, xnT, last_use):
                if not first(b):
                    act.wait_ge(*last_use)
                for h in range(2):
                    act.wait_ge(turned[n], 2 * b + h + 1)
                    s.activation(xnT[:, h * HALF:(h + 1) * HALF], xbank[h][:, :],
                                 ACT.Identity).then_inc(xnT_ready[n], 1)

            def queries_keys(b):
                if not first(b):
                    act.wait_ge(qk_ready, NG * b)
                for c, dst in enumerate((qT, kT)):
                    for h in range(2):
                        act.wait_ge(qk_filled, 4 * b + 2 * c + h + 1)
                        s.activation(dst[:, h * HALF:(h + 1) * HALF], xbank[h][:, :], ACT.Identity,
                                     bias=bias_cols[:, c:c + 1]).then_inc(qk_loaded, 1)

            def values(b):
                if not first(b):
                    act.wait_ge(wv_ready, NS * b)
                for h in range(2):
                    act.wait_ge(v_filled, 2 * b + h + 1)
                    s.activation(vT[:, PAD + h * HALF:PAD + (h + 1) * HALF], xbank[h][:, :],
                                 ACT.Identity, bias=bias_cols[:, 2:3],
                                 accum_out=v_parts[:, h:h + 1]).then_inc(v_loaded, 1)

            def exponent(b):
                act.wait_ge(shifted, b + 1)
                s.activation(es[:, :, :], es[:, :, :], ACT.Exp, scale=SCALE).then_inc(exp_ready, 1)

            def high_parts(b):
                act.wait_ge(wt_ready, b + 1)
                if not first(b):
                    act.wait_ge(spread_ready, NS * b)
                s.activation(wt_hi[:, :, :], wt[:, :, :], ACT.Identity).then_inc(hi_ready, 1)

            def attention_rows(b):
                if not first(b):
                    act.wait_ge(x1_ready, b)
                for h in range(2):
                    act.wait_ge(attn_filled, 2 * b + h + 1)
                    s.activation(attn[:, 4 * h:4 * h + 4, :], bank_rows(h), ACT.Identity)\
                        .then_inc(attn_ready, 1)

            def hidden(b, h):
                if not first(b) and h == 0:
                    act.wait_ge(y_filled, 2 * b)
                part = [hid[:, f, h * HALF:(h + 1) * HALF] for f in range(FB)]
                at = 2 * FB * b + FB * h
                for f in range(FB + 1):
                    if f < FB:
                        act.wait_ge(fc_filled, at + f + 1)
                        s.activation(part[f], xbank[f % NX][:, :], ACT.Relu).then_inc(relu_ready, 1)
                    if f >= 1:
                        act.wait_ge(relu_ready, at + f)
                        s.activation(part[f - 1], part[f - 1], ACT.Square).then_inc(hid_ready, 1)

            def outputs(b):
                if not first(b):
                    act.wait_ge(spike_step, 2 * STEPS * b)
                for h in range(2):
                    act.wait_ge(y_filled, 2 * b + h + 1)
                    s.activation(y_sb[:, 4 * h:4 * h + 4, :], bank_rows(h), ACT.Identity)\
                        .then_inc(y_ready, 1)

            def front(b):
                norm("in", b, x_all[:, b, :, :], xn_in)
                transposed("in", b, xnT_in, (v_filled, 2 * b))
                queries_keys(b)

            def step(b, before, after):
                values(b)
                if before:
                    attention_rows(b - 1)
                    norm("mid", b - 1, attn, attn)
                    norm("ff", b - 1, x_all[:, b - 1, :, :], xn_ff)
                    transposed("ff", b - 1, xnT_ff, (fc_filled, 2 * FB * (b - 1)))
                exponent(b)
                if before:
                    hidden(b - 1, 0)
                high_parts(b)
                if before:
                    hidden(b - 1, 1)
                    outputs(b - 1)
                if after:
                    front(b + 1)
                if before:
                    norm("out", b - 1, spikes, spikes)

            act.wait_ge(weights_in, 16 * NLOADS)
            front(0)
            step(0, False, True)
            for b in range(1, B - 1):
                step(b, True, True)
            step(B - 1, True, False)
            attention_rows(B - 1)
            norm("mid", B - 1, attn, attn)
            norm("ff", B - 1, x_all[:, B - 1, :, :], xn_ff)
            transposed("ff", B - 1, xnT_ff, (fc_filled, 2 * FB * (B - 1)))
            hidden(B - 1, 0)
            hidden(B - 1, 1)
            outputs(B - 1)
            norm("out", B - 1, spikes, spikes)

        @block.vector
        def _(dve):
            v = nc.vector

            def moments(n, b, src, eps):
                if not first(b):
                    dve.wait_ge(ln_mom[n], b)
                for i in range(TB):
                    last = v.bn_stats(sums[n][:, i, :], src[:, i, :])
                last.then_inc(ln_sums[n], 1)
                dve.wait_ge(ln_sums[n], b + 1)
                if not first(b):
                    dve.wait_ge(ln_var[n], b)
                for i in range(TB):
                    last = v.bn_aggr(mom[n][:, i, :], sums[n][:, i, :])
                last.then_inc(ln_mom[n], 1)
                dve.wait_ge(ln_mom[n], b + 1)
                if not first(b):
                    dve.wait_ge(ln_shift[n], b)
                v.tensor_scalar(neg_mean[n][:, :], mom[n][:, :, 0], -1.0, None, ALU.mult)
                v.tensor_scalar(var_eps[n][:, :], mom[n][:, :, 1], eps, None, ALU.add)\
                    .then_inc(ln_var[n], 1)

            def products(b, g):
                if g == 0:
                    dve.wait_ge(qk_loaded, 4 * b + 4)
                if not first(b):
                    dve.wait_ge(scores_ready, NG * (b - 1) + g + 1)
                for k in GROUPS[g]:
                    o = OFFSETS[k]
                    last = v.tensor_tensor(out=qk[:, k, o:L], in0=qT[:, o:L], in1=kT[:, 0:L - o],
                                           op=ALU.mult)
                last.then_inc(qk_ready, 1)

            def shift_scores(b):
                dve.wait_ge(scores_ready, NG * b + NG)
                v.tensor_reduce(s_max[:, :], scores[:, :, :].rearrange("p k t -> p t k"), AX.X,
                                ALU.max).then_inc(max_ready, 1)
                dve.wait_ge(max_ready, b + 1)
                if not first(b):
                    dve.wait_ge(wt_ready, b)
                v.tensor_tensor(out=es[:, :, :], in0=scores[:, :, :],
                                in1=s_max[:, :].unsqueeze(1).to_broadcast([P, SLOTS, P]),
                                op=ALU.subtract).then_inc(shifted, 1)

            def inverse(b):
                dve.wait_ge(exp_ready, b + 1)
                v.tensor_reduce(s_sum[:, :], es[:, 0:NK, :].rearrange("p k t -> p t k"), AX.X,
                                ALU.add).then_inc(sum_ready, 1)
                dve.wait_ge(sum_ready, b + 1)
                v.scalar_tensor_tensor(out=s_sum[:, :], in0=es[:, BASE, :], scalar=float(L - NK),
                                       in1=s_sum[:, :], op0=ALU.mult, op1=ALU.add).then_inc(z_ready, 1)
                dve.wait_ge(z_ready, b + 1)
                if not first(b):
                    dve.wait_ge(wt_ready, b)
                v.reciprocal(z_inv[:, :], s_sum[:, :]).then_inc(inv_ready, 1)

            def value_total(b):
                dve.wait_ge(v_loaded, 2 * b + 2)
                v.tensor_tensor(out=v_total[:, :], in0=v_parts[:, 0:1], in1=v_parts[:, 1:2],
                                op=ALU.add).then_inc(v_summed, 1)

            def weighted_values(b):
                dve.wait_ge(v_loaded, 2 * b + 2)
                if not first(b):
                    dve.wait_ge(attn_filled, 2 * b)
                for n, (slots, t0, blocks) in enumerate(SPREADS):
                    dve.wait_ge(spread_ready, NS * b + n + 1)
                    lo, hi = t0 * P, (t0 + blocks) * P
                    k, bank = slots[0], wbank[n % NW]
                    if len(slots) == 2:
                        back = vT[:, PAD + lo - OFFSETS[k]:PAD + hi - OFFSETS[k]]
                        both = two_offsets(back, OFFSETS[k] - OFFSETS[k + 1])
                        last = v.tensor_tensor(out=wv[:, k:k + 2, lo:hi],
                                               in0=bank[:, :].rearrange("p (k t) -> p k t", k=2),
                                               in1=both, op=ALU.mult)
                    elif k != BASE:
                        last = v.tensor_tensor(out=wv[:, k, lo:hi], in0=bank[:, 0:hi - lo],
                                               in1=vT[:, PAD + lo - OFFSETS[k]:PAD + hi - OFFSETS[k]],
                                               op=ALU.mult)
                    elif lo < PAD:
                        dve.wait_ge(v_summed, b + 1)
                        last = v.tensor_scalar(wv[:, NK - 1, lo:hi], bank[:, :], v_total[:, 0:1], None,
                                               ALU.mult)
                    else:
                        dve.wait_ge(wv_ready, NS * b + NS - TB // 4)
                        last = v.scalar_tensor_tensor(out=wv[:, NK - 1, lo:hi], in0=bank[:, :],
                                                      scalar=v_total[:, 0:1], in1=wv[:, NK - 1, lo:hi],
                                                      op0=ALU.mult, op1=ALU.add)
                    last.then_inc(wv_ready, 1)

            def count_spikes(b):
                if not first(b):
                    dve.wait_ge(out_ready, b)
                for n, threshold in enumerate(THRESHOLDS):
                    for h in range(2):
                        y, c = y_sb[:, 4 * h:4 * h + 4, :], spikes[:, 4 * h:4 * h + 4, :]
                        if n == 0:
                            dve.wait_ge(y_ready, 2 * b + h + 1)
                            last = v.tensor_scalar(c, y, threshold, None, ALU.is_gt)
                        else:
                            dve.wait_ge(spike_step, 2 * STEPS * b + 2 * n - 1 + h)
                            last = v.scalar_tensor_tensor(out=c, in0=y, scalar=threshold, in1=c,
                                                          op0=ALU.is_gt, op1=ALU.add)
                        last.then_inc(spike_step, 1)

            def mid_moments(b):
                dve.wait_ge(attn_ready, 2 * b + 2)
                moments("mid", b, attn, EPS)

            def ff_moments(b):
                dve.wait_ge(x1_ready, b + 1)
                moments("ff", b, x_all[:, b, :, :], EPS)

            def in_moments(b):
                dve.wait_ge(x_in, 16 * (b + 1))
                moments("in", b, x_all[:, b, :, :], EPS)

            def out_moments(b):
                dve.wait_ge(spike_step, 2 * STEPS * (b + 1))
                moments("out", b, spikes, EPS * STEPS ** 2)

            def step(b, before, after):
                products(b, 0)
                if before:
                    mid_moments(b - 1)
                products(b, 1)
                if before:
                    ff_moments(b - 1)
                products(b, 2)
                shift_scores(b)
                value_total(b)
                inverse(b)
                if after:
                    in_moments(b + 1)
                weighted_values(b)
                if before:
                    count_spikes(b - 1)
                    out_moments(b - 1)

            in_moments(0)
            v.memset(vT[:, 0:PAD], 0.0)
            for k in range(1, NK):
                v.memset(qk[:, k, 0:OFFSETS[k]], 0.0)
            v.memset(scores[:, BASE, :], 0.0).then_inc(dve_set, 1)
            dve.wait_ge(pool_set, 4)
            dve.wait_ge(bo_in, 16)
            v.tensor_copy(spread_r[:, :, :], spread[:, :, :])
            v.tensor_copy(first_row_r[:, :], first_row[:, :])
            v.tensor_copy(bo_hi[:, :], bo_row[:, :]).then_inc(dve_set, 1)
            dve.wait_ge(dve_set, 2)
            v.tensor_tensor(out=bo_lo[:, :], in0=bo_row[:, :], in1=bo_hi[:, :].bitcast(F32),
                            op=ALU.subtract).then_inc(dve_set, 1)
            step(0, False, True)
            for b in range(1, B - 1):
                step(b, True, True)
            step(B - 1, True, False)
            mid_moments(B - 1)
            ff_moments(B - 1)
            count_spikes(B - 1)
            out_moments(B - 1)

        @block.tensor
        def _(pe):
            t = nc.tensor

            def emptied(before, h):
                if before is not None:
                    pe.wait_ge(before[0], before[1] - 1 + h)

            def turn(n, b, src, before):
                for h in range(2):
                    pe.wait_ge(ln_done[n], 2 * b + h + 1)
                    emptied(before, h)
                    for i in range(4):
                        last = t.transpose(xbank[h][:, i * P:(i + 1) * P], src[:, 4 * h + i, :],
                                           ident[:, :])
                    last.then_inc(turned[n], 1)

            def project(w, xnT, ready, filled, at, before):
                for h in range(2):
                    pe.wait_ge(ready[0], ready[1] + h + 1)
                    emptied(before, h)
                    t.matmul(xbank[h][:, :], w, xnT[:, h * HALF:(h + 1) * HALF], start=True,
                             stop=True).then_inc(filled, 1)

            def queries_keys(b):
                ready = (xnT_ready["in"], 2 * b)
                project(wq_sb[:, :], xnT_in, ready, qk_filled, b, (xnT_ready["in"], 2 * b + 2))
                project(wk_sb[:, :], xnT_in, ready, qk_filled, b, (qk_loaded, 4 * b + 2))

            def values(b):
                project(wv_sb[:, :], xnT_in, (xnT_ready["in"], 2 * b), v_filled, b,
                        (qk_loaded, 4 * b + 4))

            def score(b, g):
                pe.wait_ge(qk_ready, NG * b + g + 1)
                if not first(b) and g == 0:
                    pe.wait_ge(shifted, b)
                k0, k1 = GROUPS[g][0], GROUPS[g][-1] + 1
                for half in range(2):
                    for j in range(4):
                        tok = (2 * j + half) * P
                        last = t.matmul(scores[32 * j:32 * j + 32, k0:k1, :], head_sum[:, half, :],
                                        qk[:, k0:k1, tok:tok + P], start=half == 0, stop=half == 1)
                last.then_inc(scores_ready, 1)

            def spread_weights(b):
                pe.wait_ge(hi_ready, b + 1)
                pe.wait_ge(lo_ready, b + 1)
                for n, (slots, t0, blocks) in enumerate(SPREADS):
                    if not first(b) or n >= NW:
                        pe.wait_ge(wv_ready, NS * b + n - NW + 1)
                    ks = slice(slots[0], slots[-1] + 1)
                    bank = wbank[n % NW][:, 0:len(slots) * blocks * P]\
                        .rearrange("p (k t) -> p k t", k=len(slots))
                    for i in range(blocks):
                        for part, start in ((wt_hi, True), (wt_lo, False)):
                            last = t.matmul(bank[:, :, i * P:(i + 1) * P], spread_r[:, t0 + i, :],
                                            part[:, ks, :], start=start, stop=not start)
                    last.then_inc(spread_ready, 1)

            def attention_out(b, before):
                pe.wait_ge(merged, NM * b + NM)
                pe.wait_ge(wv_ready, NS * b + NS)
                for h in range(2):
                    emptied(before, h)
                    for part, start in ((bo_hi, True), (bo_lo, False)):
                        t.matmul(bank_rows(h), first_row_r[:, :],
                                 part[:, :].unsqueeze(1).to_broadcast([P, 4, D]),
                                 start=start, stop=False)
                    for i in range(4):
                        tok = (4 * h + i) * P
                        for k in (0, 1, NK - 1):
                            last = t.matmul(xbank[h][:, i * P:(i + 1) * P], wv[:, k, tok:tok + P],
                                            wo_sb[:, :], start=False, stop=i == 3 and k == NK - 1)
                    last.then_inc(attn_filled, 1)

            def feed_forward_in(b):
                for h in range(2):
                    pe.wait_ge(xnT_ready["ff"], 2 * b + 2)
                    for f in range(FB):
                        n = FB * h + f
                        if n >= NX:
                            pe.wait_ge(relu_ready, 2 * FB * b + n - NX + 1)
                        t.matmul(xbank[n % NX][:, :], wfc_sb[:, f * P:(f + 1) * P],
                                 xnT_ff[:, h * HALF:(h + 1) * HALF], start=True,
                                 stop=True).then_inc(fc_filled, 1)

            def feed_forward_out(b):
                for h in range(2):
                    pe.wait_ge(hid_ready, 2 * FB * b + FB * (h + 1))
                    emptied((relu_ready, 2 * FB * (b + 1)), h)
                    for i in range(4):
                        tok = (4 * h + i) * P
                        for f in range(FB):
                            last = t.matmul(xbank[h][:, i * P:(i + 1) * P], hid[:, f, tok:tok + P],
                                            wproj_sb[:, f, :], start=f == 0, stop=f == FB - 1)
                    last.then_inc(y_filled, 1)

            def step(b, before, after):
                values(b)
                if before:
                    attention_out(b - 1, (v_loaded, 2 * b + 2))
                for g in range(NG):
                    score(b, g)
                if before:
                    turn("ff", b - 1, xn_ff, (attn_ready, 2 * b))
                    feed_forward_in(b - 1)
                    feed_forward_out(b - 1)
                if after:
                    turn("in", b + 1, xn_in,
                         (y_ready, 2 * b) if before else (v_loaded, 2 * b + 2))
                    queries_keys(b + 1)
                spread_weights(b)

            pe.wait_ge(pool_set, 4)
            turn("in", 0, xn_in, None)
            pe.wait_ge(weights_in, 16 * NLOADS)
            queries_keys(0)
            pe.wait_ge(dve_set, 3)
            step(0, False, True)
            for b in range(1, B - 1):
                step(b, True, True)
            step(B - 1, True, False)
            attention_out(B - 1, (y_ready, 2 * B - 2))
            turn("ff", B - 1, xn_ff, (attn_ready, 2 * B))
            feed_forward_in(B - 1)
            feed_forward_out(B - 1)


def kernel(L0_attn_x, L0_attn_Wq, L0_attn_bq, L0_attn_Wk, L0_attn_bk, L0_attn_Wv, L0_attn_bv,
           L0_attn_Wo, L0_attn_bo, L0_ffn_W_fc, L0_ffn_W_proj):
    import concourse.bacc as bacc
    from concourse.bass_utils import run_bass_kernel_spmd

    col = lambda a: np.asarray(a).reshape(-1, 1)
    laid = {
        "x": np.asarray(L0_attn_x),
        "wq_t": np.asarray(L0_attn_Wq).T, "bq": col(L0_attn_bq),
        "wk_t": np.asarray(L0_attn_Wk).T, "bk": col(L0_attn_bk),
        "wv_t": np.asarray(L0_attn_Wv).T, "bv": col(L0_attn_bv),
        "wo_t": np.asarray(L0_attn_Wo).T, "bo": np.asarray(L0_attn_bo).reshape(1, -1),
        "wfc_t": np.asarray(L0_ffn_W_fc).T, "wproj_t": np.asarray(L0_ffn_W_proj).T,
    }
    laid = {n: np.ascontiguousarray(a) for n, a in laid.items()}
    nc = bacc.Bacc("TRN2", target_bir_lowering=False, num_devices=1)
    args = [nc.dram_tensor(n, a.shape, F32, kind="ExternalInput").ap() for n, a in laid.items()]
    out = nc.dram_tensor("out", laid["x"].shape, F32, kind="ExternalOutput").ap()
    log_sparse_block(nc, *args, out)
    result = run_bass_kernel_spmd(nc, [laid], core_ids=[0])
    return result.results[0]["out"]
```

```python
from contextlib import ExitStack

import numpy as np

import concourse.bass as bass
from concourse import mybir

F32 = mybir.dt.float32
F32R = mybir.dt.float32r
ALU = mybir.AluOpType
ACT = mybir.ActivationFunctionType
AX = mybir.AxisListType

BETA, THRESHOLD, STEPS = 0.9, 1.0, 5
EPS = 1e-5
P = 128


PE_ORDER = [
    ("down", -2, 0), ("spread", -1, 0), ("turn ff", -2, 1), ("spread", -1, 1), ("attention", -1, 0),
    ("values", 0, 0), ("up", -2, 1), ("scores", 0, 0), ("scores", 0, 1), ("attention", -1, 1),
    ("scores", 0, 2), ("turn in", 1, 0), ("down", -2, 1), ("turn ff", -1, 0), ("turn in", 1, 1),
    ("queries", 1, 0), ("keys", 1, 0), ("up", -1, 0)]
ACT_ORDER = [
    ("norm ff", -2, 1), ("outputs", -2, 0), ("turned ff", -2, 1), ("attention", -1, 0),
    ("values", 0, 0), ("hidden", -2, 1), ("norm mid", -1, 0), ("norm in", 1, 0),
    ("attention", -1, 1), ("norm out", -2, 0), ("norm in", 1, 1), ("norm ff", -1, 0),
    ("turned in", 1, 0), ("outputs", -2, 1), ("turned ff", -1, 0), ("turned in", 1, 1),
    ("norm mid", -1, 1), ("exp", 0, 0), ("queries, keys", 1, 0), ("hidden", -1, 0),
    ("norm out", -2, 1), ("rounded", 0, 0), ("rounded", 0, 1)]
DVE_ORDER = [
    ("moments in", 1, 0), ("inverse", -1, 0), ("moments ff", -2, 1), ("products", 0, 0),
    ("rests", -1, 0), ("weights * v", -1, 0), ("weights * v", -1, 1), ("products", 0, 1),
    ("moments mid", -1, 0), ("spikes", -2, 0), ("products", 0, 2), ("moments in", 1, 1),
    ("sum of v", 0, 0), ("moments out", -2, 0), ("moments ff", -1, 0), ("moments mid", -1, 1),
    ("max and shift", 0, 0), ("spikes", -2, 1), ("moments out", -2, 1)]
POOL_ORDER = [
    ("rsqrt in", 1, 0), ("rsqrt out", -2, 0), ("rsqrt in", 1, 1), ("rsqrt ff", -1, 0),
    ("final", -2, 0), ("rsqrt mid", -1, 1), ("residual", -1, 1), ("differences", 0, 0),
    ("rsqrt out", -2, 1), ("normalise", 0, 0), ("rests", 0, 1), ("rsqrt ff", -1, 1),
    ("merge", 0, 0), ("merge", 0, 1), ("rsqrt mid", 0, 0), ("final", -2, 1), ("residual", 0, 0)]
BANKS = {"values": 2, "queries": 2, "keys": 2, "turn in": 1, "turn ff": 1, "attention": 1,
         "up": 4, "down": 1}


def spikes_of(y):
    y = np.float32(y)
    mem, spikes = np.float32(0), 0
    for _ in range(STEPS):
        reset = np.float32(mem - np.float32(THRESHOLD) > 0)
        mem = np.float32(np.float32(np.float32(BETA) * mem) + y) - reset * np.float32(THRESHOLD)
        spikes += int(mem - np.float32(THRESHOLD) > 0)
    return spikes


def spike_thresholds():
    found = []
    for n in range(STEPS):
        low, high = np.float32(0), np.float32(2 * THRESHOLD)
        while np.nextafter(low, high) < high:
            middle = np.float32((low + high) / 2)
            if middle in (low, high):
                middle = np.nextafter(low, high)
            low, high = (middle, high) if spikes_of(middle) <= n else (low, middle)
        found.append(float(low))
    return found


def log_sparse_block(nc, x, wq_t, bq, wk_t, bk, wv_t, bv, wo_t, bo, wfc_t, wproj_t, out):
    B, L, D = x.shape
    H = 16
    HD = D // H
    FF = wfc_t.shape[1]
    FB = FF // P
    TB = L // P
    HALF = L // 2
    OFFSETS = [0] + [1 << k for k in range(L.bit_length() - 1)]
    NK = len(OFFSETS)
    SLOTS = NK + 1
    BASE = NK
    PAD = OFFSETS[-1]
    SCALE = 1.0 / float(np.sqrt(HD))
    GROUPS = [range(g, min(g + 4, NK)) for g in range(0, NK, 4)]
    PAIRS = [(k, k + 1) for k in range(0, NK - 1, 2)]
    THRESHOLDS = spike_thresholds()
    SPREADS = []
    for h in range(2):
        t0, t1 = h * TB // 2, (h + 1) * TB // 2
        SPREADS.append([(pair, t, 2) for pair in PAIRS for t in range(t0, t1, 2)]
                       + [((NK - 1,), t, 2) for t in range(t0, t1, 2) if t * P >= PAD]
                       + [((BASE,), t0, TB // 2)])
    NW = 3
    NX = 2
    S0, NS = len(SPREADS[0]), len(SPREADS[0]) + len(SPREADS[1])
    assert D == P and L == 1024 and NS % NW == 0 and SLOTS * P == 3 * 512

    x_rows = x.rearrange("b (i p) d -> b p i d", p=P)
    out_rows = out.rearrange("b (i p) d -> b p i d", p=P)

    ctx = ExitStack()
    with ctx:
        def sb(name, shape, dt=F32):
            return ctx.enter_context(nc.sbuf_tensor(name, shape, dt))

        def pb(name, shape, dt=F32):
            return ctx.enter_context(nc.psum_tensor(name, shape, dt))

        def sem(name):
            return ctx.enter_context(nc.semaphore(name))

        wq_sb, wk_sb, wv_sb, wo_sb = (sb(n, [P, D]) for n in ("wq_sb", "wk_sb", "wv_sb", "wo_sb"))
        wfc_sb = sb("wfc_sb", [P, FF])
        wproj_sb = sb("wproj_sb", [P, FB, D])
        bias_cols = sb("bias_cols", [P, 3])
        bo_row = sb("bo_row", [P, D])
        bo_hi, bo_lo = sb("bo_hi", [P, D], F32R), sb("bo_lo", [P, D], F32R)
        first_row = sb("first_row", [P, P])
        first_row_r = sb("first_row_r", [P, P], F32R)
        ident = sb("ident", [P, P])
        head_sum = sb("head_sum", [P, 2, 32])
        spread = sb("spread", [P, TB // 2, P])
        spread_r = sb("spread_r", [P, TB // 2, P], F32R)
        neg_half = sb("neg_half", [P, TB])
        warm = sb("warm", [P, 1])
        x_all = sb("x_all", [P, B, TB, D])
        xn_in, xn_ff = sb("xn_in", [P, TB, D]), sb("xn_ff", [P, TB, D])
        xnT_in, xnT_ff = sb("xnT_in", [P, L]), sb("xnT_ff", [P, L])
        qT, kT = sb("qT", [P, L]), sb("kT", [P, L])
        vT = sb("vT", [P, PAD + L])
        v_parts = sb("v_parts", [P, 2])
        v_total = sb("v_total", [P, 1])
        qk = sb("qk", [P, NK, L])
        wv = sb("wv", [P, NK, L])
        s_max, s_sum, z_inv = sb("s_max", [P, P]), sb("s_sum", [P, P]), sb("z_inv", [P, P])
        es = sb("es", [P, SLOTS, P])
        wt = sb("wt", [P, SLOTS, P])
        wt_parts = sb("wt_parts", [P, 2, SLOTS, P], F32R)
        attn = sb("attn", [P, TB, D])
        hid = sb("hid", [P, FB, L])
        y_sb = sb("y_sb", [P, TB, D])
        spikes = sb("spikes", [P, TB, D])
        LN = ("in", "mid", "ff", "out")
        sums = {n: sb(f"sums_{n}", [P, TB, 6]) for n in LN}
        mom = {n: sb(f"mom_{n}", [P, TB, 2]) for n in LN}
        neg_mean = {n: sb(f"neg_mean_{n}", [P, TB]) for n in LN}
        var_eps = {n: sb(f"var_eps_{n}", [P, TB]) for n in LN}
        rstd = {n: sb(f"rstd_{n}", [P, TB]) for n in LN}
        shift = {n: sb(f"shift_{n}", [P, TB]) for n in LN}
        scores = pb("scores", [P, SLOTS, P])
        wbank = [pb(f"wbank{i}", [P, 512]) for i in range(NW)]
        xbank = [pb(f"xbank{i}", [P, 512]) for i in range(NX)]

        NG = len(GROUPS)
        MERGES = [(0, 2, 2), (4, 6, 4), (0, 4, 4), (0, 8, 5)]
        NM = len(MERGES)
        EARLY = [(wq_sb[:, :], wq_t), (wk_sb[:, :], wk_t), (bias_cols[:, 0:1], bq), (bias_cols[:, 1:2], bk),
                 (bias_cols[:, 2:3], bv), (wv_sb[:, :], wv_t), (wo_sb[:, :], wo_t)]

        def first(b):
            return b == 0

        def steps(order):
            lags = [lag for _, lag, _ in order]
            return [[(stage, step + lag, part) for stage, lag, part in order if 0 <= step + lag < B]
                    for step in range(-max(lags), B - min(lags))]

        fills_before, filled = {}, 0
        for step in steps(PE_ORDER):
            for stage, b, part in step:
                fills_before[stage, b, part] = filled
                filled += BANKS.get(stage, 0)

        def fill(stage, b, h=0):
            return fills_before[stage, b, h]

        def fill_bank(stage, b, h=0):
            return fill(stage, b, h) % NX

        def run(order, stages, constants=None):
            for n, step in enumerate(steps(order)):
                if n == 1 and constants:
                    constants()
                for stage, b, part in step:
                    stages[stage](b, part)

        def per_slot(row):
            return row.unsqueeze(1).to_broadcast([P, NK, P])

        def rows_of(bank):
            return xbank[bank][:, :].rearrange("p (i d) -> p i d", d=D)

        def packed_rows(packed, h):
            return packed[h * P // 2:(h + 1) * P // 2, :, :]

        def rounded_rows(h):
            return wt_parts[h * P // 2:(h + 1) * P // 2, h, :, :]

        def rest_rows(h):
            return wt_parts[(1 - h) * P // 2:(2 - h) * P // 2, h, :, :]

        def half_rows(h):
            return slice(4 * h, 4 * h + 4)

        def two_offsets(tokens, step):
            partitions, run = tokens.ap
            return bass.AP(tensor=tokens.tensor, offset=tokens.offset,
                           ap=[list(partitions), [step, 2], list(run)])

        early_in, late_in, bo_in = sem("early_in"), sem("late_in"), sem("bo_in")
        x_first = [sem("x_first_0"), sem("x_first_1")]
        x_in, stored = sem("x_in"), sem("stored")
        pool_set, dve_set = sem("pool_set"), sem("dve_set")
        ln_sums = {n: sem(f"ln_sums_{n}") for n in LN}
        ln_mom = {n: sem(f"ln_mom_{n}") for n in LN}
        ln_var = {n: sem(f"ln_var_{n}") for n in LN}
        ln_rstd = {n: sem(f"ln_rstd_{n}") for n in LN}
        ln_shift = {n: sem(f"ln_shift_{n}") for n in LN}
        ln_done = {n: sem(f"ln_done_{n}") for n in LN}
        x_filled, x_emptied = sem("x_filled"), sem("x_emptied")
        hid_ready = sem("hid_ready")
        v_summed = sem("v_summed")
        qk_ready = sem("qk_ready")
        scores_ready = sem("scores_ready")
        max_ready, shifted, exp_ready = sem("max_ready"), sem("shifted"), sem("exp_ready")
        sum_ready, z_ready, inv_ready = sem("sum_ready"), sem("z_ready"), sem("inv_ready")
        diff_ready, wt_ready = sem("diff_ready"), sem("wt_ready")
        hi_ready = sem("hi_ready")
        lo_ready = [sem("lo_ready_0"), sem("lo_ready_1")]
        spread_ready = sem("spread_ready")
        wv_ready = sem("wv_ready")
        merged = sem("merged")
        x1_ready, out_ready = sem("x1_ready"), sem("out_ready")
        spike_step = sem("spike_step")

        block = ctx.enter_context(nc.Block())

        @block.sync
        def _(sp):
            for h in range(2):
                sp.dma_start(x_all[:, 0, half_rows(h), :], x_rows[0, :, half_rows(h), :])\
                    .then_inc(x_first[h], 16)
            sp.dma_start(wfc_sb[:, :], wfc_t).then_inc(late_in, 16)
            sp.dma_start(wproj_sb[:, :, :], wproj_t.rearrange("(f p) d -> p f d", p=P))\
                .then_inc(late_in, 16)
            sp.wait_ge(pool_set, 1)
            sp.dma_start(bo_row[0:1, :], bo).then_inc(bo_in, 16)
            for b in range(1, B):
                if b >= 2:
                    sp.wait_ge(x_in, 16 * (b - 1))
                sp.dma_start(x_all[:, b, :, :], x_rows[b, :, :, :]).then_inc(x_in, 16)
            for b in range(B):
                for h in range(2):
                    sp.wait_ge(out_ready, 2 * b + h + 1)
                    sp.dma_start(out_rows[b, :, half_rows(h), :], x_all[:, b, half_rows(h), :])\
                        .then_inc(stored, 16)
            sp.wait_ge(stored, 16 * 2 * B)

        @block.gpsimd
        def _(pool):
            g = nc.gpsimd
            g.memset(warm[:, :], 0.0)
            g.memset(bo_row[:, :], 0.0).then_inc(pool_set, 1)
            g.memset(ident[:, :], 0.0)
            g.memset(first_row[:, :], 0.0)
            g.memset(head_sum[:, :, :], 1.0)
            g.memset(spread[:, :, :], 0.0)
            g.memset(neg_half[:, :], -0.5).then_inc(pool_set, 1)
            pool.wait_ge(pool_set, 2)
            g.affine_select(out=ident[:, :], in_=ident[:, :], compare_op=ALU.not_equal, fill=1.0,
                            base=0, pattern=[[-1, P]], channel_multiplier=1)
            g.affine_select(out=first_row[:, :], in_=first_row[:, :], compare_op=ALU.not_equal,
                            fill=1.0, base=0, pattern=[[0, P]], channel_multiplier=1)
            g.affine_select(out=head_sum[:, :, :], in_=head_sum[:, :, :], compare_op=ALU.is_ge,
                            fill=0.0, base=0, pattern=[[HD * H, 2], [-HD, 2 * H]],
                            channel_multiplier=1).then_inc(pool_set, 1)
            pool.wait_ge(pool_set, 3)
            g.affine_select(out=head_sum[:, :, :], in_=head_sum[:, :, :], compare_op=ALU.is_ge,
                            fill=0.0, base=HD - 1, pattern=[[-HD * H, 2], [HD, 2 * H]],
                            channel_multiplier=-1).then_inc(pool_set, 1)
            def rsqrt(n, b, h):
                pool.wait_ge(ln_var[n], 2 * b + h + 1)
                if not first(b):
                    pool.wait_ge(ln_done[n], 2 * b + h - 1)
                r = half_rows(h)
                g.tensor_tensor(out=rstd[n][:, r], in0=var_eps[n][:, r], in1=neg_half[:, r],
                                op=ALU.pow).then_inc(ln_rstd[n], 1)
                pool.wait_ge(ln_rstd[n], 2 * b + h + 1)
                g.tensor_tensor(out=shift[n][:, r], in0=neg_mean[n][:, r], in1=rstd[n][:, r],
                                op=ALU.mult).then_inc(ln_shift[n], 1)

            def differences(b, h):
                pool.wait_ge(exp_ready, b + 1)
                if not first(b):
                    pool.wait_ge(lo_ready[0], b)
                    pool.wait_ge(lo_ready[1], b)
                g.tensor_tensor(out=wt[:, 0:NK, :], in0=es[:, 0:NK, :], in1=per_slot(es[:, BASE, :]),
                                op=ALU.subtract).then_inc(diff_ready, 1)

            def normalise(b, h):
                pool.wait_ge(inv_ready, b + 1)
                pool.wait_ge(diff_ready, b + 1)
                g.tensor_tensor(out=wt[:, BASE, :], in0=es[:, BASE, :], in1=z_inv[:, :], op=ALU.mult)
                g.tensor_tensor(out=wt[:, 0:NK, :], in0=wt[:, 0:NK, :], in1=per_slot(z_inv[:, :]),
                                op=ALU.mult).then_inc(wt_ready, 1)

            def low_parts(b, h):
                pool.wait_ge(hi_ready, 2 * b + h + 1)
                if not first(b):
                    pool.wait_ge(spread_ready, NS * (b - 1) + (NS if h else S0))
                g.tensor_tensor(out=rest_rows(h), in0=packed_rows(wt, h),
                                in1=rounded_rows(h).bitcast(F32),
                                op=ALU.subtract).then_inc(lo_ready[h], 1)
                pool.wait_ge(lo_ready[h], b + 1)

            def merge(b, h):
                tok = slice(h * HALF, (h + 1) * HALF)
                for n, (into, other, pairs) in enumerate(MERGES):
                    pool.wait_ge(wv_ready, NS * b + S0 * h + 2 * pairs)
                    if n >= 2:
                        pool.wait_ge(merged, NM * (2 * b + h) + n)
                    g.tensor_tensor(out=wv[:, into:into + 2, tok], in0=wv[:, into:into + 2, tok],
                                    in1=wv[:, other:other + 2, tok], op=ALU.add).then_inc(merged, 1)

            def residual(b, h):
                pool.wait_ge(ln_done["mid"], 2 * b + h + 1)
                r = half_rows(h)
                g.tensor_tensor(out=x_all[:, b, r, :], in0=x_all[:, b, r, :], in1=attn[:, r, :],
                                op=ALU.add).then_inc(x1_ready, 1)

            def final(b, h):
                pool.wait_ge(ln_done["out"], 2 * b + h + 1)
                r = half_rows(h)
                g.tensor_tensor(out=x_all[:, b, r, :], in0=x_all[:, b, r, :], in1=spikes[:, r, :],
                                op=ALU.add).then_inc(out_ready, 1)

            def constants():
                for half in range(2):
                    for t in range(TB // 2):
                        part = spread[:, t, :].rearrange("p (h d) -> p h d", d=HD)
                        last = g.affine_select(out=part, in_=part, compare_op=ALU.not_equal, fill=1.0,
                                               base=-H * t - half * P // 2, pattern=[[-1, H], [0, HD]],
                                               channel_multiplier=1)
                    last.then_inc(pool_set, 1)
                    pool.wait_ge(pool_set, 5 + half)

            run(POOL_ORDER, {
                "differences": differences, "normalise": normalise, "rests": low_parts,
                "merge": merge, "residual": residual, "final": final,
                "rsqrt in": lambda b, h: rsqrt("in", b, h),
                "rsqrt mid": lambda b, h: rsqrt("mid", b, h),
                "rsqrt ff": lambda b, h: rsqrt("ff", b, h),
                "rsqrt out": lambda b, h: rsqrt("out", b, h)}, constants)

        @block.scalar
        def _(act):
            s = nc.scalar

            def empty(stage, b, h, n, dst, func=ACT.Identity, **more):
                act.wait_ge(x_filled, fill(stage, b, h) + n + 1)
                bank = (fill_bank(stage, b, h) + n) % NX
                src = rows_of(bank) if len(dst.shape) == 3 else xbank[bank][:, :]
                s.activation(dst, src, func, **more).then_inc(x_emptied, 1)

            def norm(n, b, h, src, dst):
                act.wait_ge(ln_shift[n], 2 * b + h + 1)
                for i in range(4 * h, 4 * h + 4):
                    row = s.activation(dst[:, i, :], src[:, i, :], ACT.Identity,
                                       bias=shift[n][:, i:i + 1], scale=rstd[n][:, i:i + 1])
                row.then_inc(ln_done[n], 1)

            def norm_in(b, h):
                if not first(b):
                    act.wait_ge(x_filled, fill("turn in", b - 1, h) + 1)
                norm("in", b, h, x_all[:, b, :, :], xn_in)

            def norm_ff(b, h):
                if not first(b):
                    act.wait_ge(x_filled, fill("turn ff", b - 1, h) + 1)
                norm("ff", b, h, x_all[:, b, :, :], xn_ff)

            def turned_in(b, h):
                if not first(b):
                    act.wait_ge(x_filled, fill("values", b - 1) + 2)
                empty("turn in", b, h, 0, xnT_in[:, h * HALF:(h + 1) * HALF])

            def turned_ff(b, h):
                if not first(b):
                    act.wait_ge(x_filled, fill("up", b - 1, h) + FB)
                empty("turn ff", b, h, 0, xnT_ff[:, h * HALF:(h + 1) * HALF])

            def queries_keys(b, h):
                if first(b):
                    act.wait_ge(early_in, 16 * len(EARLY))
                if not first(b):
                    act.wait_ge(qk_ready, NG * b)
                for c, (stage, dst) in enumerate((("queries", qT), ("keys", kT))):
                    for n in range(2):
                        empty(stage, b, 0, n, dst[:, n * HALF:(n + 1) * HALF],
                              bias=bias_cols[:, c:c + 1])

            def values(b, h):
                if not first(b):
                    act.wait_ge(wv_ready, NS * b)
                for n in range(2):
                    empty("values", b, 0, n, vT[:, PAD + n * HALF:PAD + (n + 1) * HALF],
                          bias=bias_cols[:, 2:3], accum_out=v_parts[:, n:n + 1])

            def exponent(b, h):
                act.wait_ge(shifted, b + 1)
                s.activation(es[:, :, :], es[:, :, :], ACT.Exp, scale=SCALE).then_inc(exp_ready, 1)

            def high_parts(b, h):
                act.wait_ge(wt_ready, b + 1)
                if not first(b):
                    act.wait_ge(spread_ready, NS * (b - 1) + (NS if h else S0))
                s.activation(rounded_rows(h), packed_rows(wt, h), ACT.Identity).then_inc(hi_ready, 1)

            def attention_rows(b, h):
                if not first(b):
                    act.wait_ge(x1_ready, 2 * b + h - 1)
                empty("attention", b, h, 0, attn[:, half_rows(h), :])

            def hidden(b, h):
                if not first(b):
                    act.wait_ge(x_filled, fill("down", b - 1, h) + 1)
                part = [hid[:, f, h * HALF:(h + 1) * HALF] for f in range(FB)]
                for f in range(FB + 1):
                    if f < FB:
                        empty("up", b, h, f, part[f], ACT.Relu)
                    if f >= 1:
                        act.wait_ge(x_emptied, fill("up", b, h) + f)
                        s.activation(part[f - 1], part[f - 1], ACT.Square).then_inc(hid_ready, 1)

            def outputs(b, h):
                if not first(b):
                    act.wait_ge(spike_step, STEPS * (2 * b + h - 1))
                empty("down", b, h, 0, y_sb[:, half_rows(h), :])

            act.wait_ge(pool_set, 1)
            s.activation(warm[:, :], warm[:, :], ACT.Exp)
            for dst, src in EARLY:
                act.dma_start(dst, src).then_inc(early_in, 16)
            run(ACT_ORDER, {
                "values": values, "queries, keys": queries_keys, "turned in": turned_in,
                "turned ff": turned_ff, "norm in": norm_in, "norm ff": norm_ff,
                "norm mid": lambda b, h: norm("mid", b, h, attn, attn),
                "norm out": lambda b, h: norm("out", b, h, spikes, spikes),
                "exp": exponent, "rounded": high_parts, "attention": attention_rows,
                "hidden": hidden, "outputs": outputs})

        @block.vector
        def _(dve):
            v = nc.vector

            def moments(n, b, h, src, eps):
                at, r = 2 * b + h + 1, half_rows(h)
                if not first(b):
                    dve.wait_ge(ln_mom[n], at - 2)
                for i in range(4 * h, 4 * h + 4):
                    last = v.bn_stats(sums[n][:, i, :], src[:, i, :])
                last.then_inc(ln_sums[n], 1)
                dve.wait_ge(ln_sums[n], at)
                if not first(b):
                    dve.wait_ge(ln_var[n], at - 2)
                for i in range(4 * h, 4 * h + 4):
                    last = v.bn_aggr(mom[n][:, i, :], sums[n][:, i, :])
                last.then_inc(ln_mom[n], 1)
                dve.wait_ge(ln_mom[n], at)
                if not first(b):
                    dve.wait_ge(ln_shift[n], at - 2)
                v.tensor_scalar(neg_mean[n][:, r], mom[n][:, r, 0], -1.0, None, ALU.mult)
                v.tensor_scalar(var_eps[n][:, r], mom[n][:, r, 1], eps, None, ALU.add)\
                    .then_inc(ln_var[n], 1)

            def products(b, g):
                if g == 0:
                    dve.wait_ge(x_emptied, fill("keys", b) + 2)
                if not first(b):
                    dve.wait_ge(scores_ready, NG * (b - 1) + g + 1)
                for k in GROUPS[g]:
                    o = OFFSETS[k]
                    last = v.tensor_tensor(out=qk[:, k, o:L], in0=qT[:, o:L], in1=kT[:, 0:L - o],
                                           op=ALU.mult)
                last.then_inc(qk_ready, 1)

            def shift_scores(b, h):
                dve.wait_ge(scores_ready, NG * b + NG)
                v.tensor_reduce(s_max[:, :], scores[:, :, :].rearrange("p k t -> p t k"), AX.X,
                                ALU.max).then_inc(max_ready, 1)
                dve.wait_ge(max_ready, b + 1)
                if not first(b):
                    dve.wait_ge(wt_ready, b)
                v.tensor_tensor(out=es[:, :, :], in0=scores[:, :, :],
                                in1=s_max[:, :].unsqueeze(1).to_broadcast([P, SLOTS, P]),
                                op=ALU.subtract).then_inc(shifted, 1)

            def inverse(b, h):
                dve.wait_ge(exp_ready, b + 1)
                v.tensor_reduce(s_sum[:, :], es[:, 0:NK, :].rearrange("p k t -> p t k"), AX.X,
                                ALU.add).then_inc(sum_ready, 1)
                dve.wait_ge(sum_ready, b + 1)
                v.scalar_tensor_tensor(out=s_sum[:, :], in0=es[:, BASE, :], scalar=float(L - NK),
                                       in1=s_sum[:, :], op0=ALU.mult, op1=ALU.add).then_inc(z_ready, 1)
                dve.wait_ge(z_ready, b + 1)
                if not first(b):
                    dve.wait_ge(wt_ready, b)
                v.reciprocal(z_inv[:, :], s_sum[:, :]).then_inc(inv_ready, 1)

            def low_parts(b, h):
                dve.wait_ge(hi_ready, 2 * b + h + 1)
                if not first(b):
                    dve.wait_ge(spread_ready, NS * (b - 1) + (NS if h else S0))
                v.tensor_tensor(out=rest_rows(h), in0=packed_rows(wt, h),
                                in1=rounded_rows(h).bitcast(F32),
                                op=ALU.subtract).then_inc(lo_ready[h], 1)

            def value_total(b, h):
                dve.wait_ge(x_emptied, fill("values", b) + 2)
                v.tensor_tensor(out=v_total[:, :], in0=v_parts[:, 0:1], in1=v_parts[:, 1:2],
                                op=ALU.add).then_inc(v_summed, 1)

            def weighted_values(b, h):
                dve.wait_ge(x_emptied, fill("values", b) + 2)
                if not first(b):
                    dve.wait_ge(x_filled, fill("attention", b - 1, h) + 1)
                done = NS * b + S0 * h
                for n, (slots, t0, blocks) in enumerate(SPREADS[h]):
                    dve.wait_ge(spread_ready, done + n + 1)
                    lo, hi = t0 * P, (t0 + blocks) * P
                    k, bank = slots[0], wbank[(S0 * h + n) % NW]
                    if len(slots) == 2:
                        back = vT[:, PAD + lo - OFFSETS[k]:PAD + hi - OFFSETS[k]]
                        both = two_offsets(back, OFFSETS[k] - OFFSETS[k + 1])
                        last = v.tensor_tensor(out=wv[:, k:k + 2, lo:hi],
                                               in0=bank[:, :].rearrange("p (k t) -> p k t", k=2),
                                               in1=both, op=ALU.mult)
                    elif k != BASE:
                        last = v.tensor_tensor(out=wv[:, k, lo:hi], in0=bank[:, 0:hi - lo],
                                               in1=vT[:, PAD + lo - OFFSETS[k]:PAD + hi - OFFSETS[k]],
                                               op=ALU.mult)
                    elif lo < PAD:
                        dve.wait_ge(v_summed, b + 1)
                        last = v.tensor_scalar(wv[:, NK - 1, lo:hi], bank[:, :], v_total[:, 0:1], None,
                                               ALU.mult)
                    else:
                        dve.wait_ge(wv_ready, done + n)
                        last = v.scalar_tensor_tensor(out=wv[:, NK - 1, lo:hi], in0=bank[:, :],
                                                      scalar=v_total[:, 0:1], in1=wv[:, NK - 1, lo:hi],
                                                      op0=ALU.mult, op1=ALU.add)
                    last.then_inc(wv_ready, 1)

            def count_spikes(b, h):
                if not first(b):
                    dve.wait_ge(out_ready, 2 * b + h - 1)
                dve.wait_ge(x_emptied, fill("down", b, h) + 1)
                y, c = y_sb[:, half_rows(h), :], spikes[:, half_rows(h), :]
                for n, threshold in enumerate(THRESHOLDS):
                    if n == 0:
                        last = v.tensor_scalar(c, y, threshold, None, ALU.is_gt)
                    else:
                        dve.wait_ge(spike_step, STEPS * (2 * b + h) + n)
                        last = v.scalar_tensor_tensor(out=c, in0=y, scalar=threshold, in1=c,
                                                      op0=ALU.is_gt, op1=ALU.add)
                    last.then_inc(spike_step, 1)

            def mid_moments(b, h):
                dve.wait_ge(x_emptied, fill("attention", b, h) + 1)
                moments("mid", b, h, attn, EPS)

            def ff_moments(b, h):
                dve.wait_ge(x1_ready, 2 * b + h + 1)
                moments("ff", b, h, x_all[:, b, :, :], EPS)

            def in_moments(b, h):
                if first(b):
                    dve.wait_ge(x_first[h], 16)
                else:
                    dve.wait_ge(x_in, 16 * b)
                moments("in", b, h, x_all[:, b, :, :], EPS)

            def out_moments(b, h):
                dve.wait_ge(spike_step, STEPS * (2 * b + h + 1))
                moments("out", b, h, spikes, EPS * STEPS ** 2)

            def constants():
                v.memset(vT[:, 0:PAD], 0.0)
                for k in range(1, NK):
                    v.memset(qk[:, k, 0:OFFSETS[k]], 0.0)
                v.memset(scores[:, BASE, :], 0.0).then_inc(dve_set, 1)
                dve.wait_ge(pool_set, 6)
                dve.wait_ge(bo_in, 16)
                v.tensor_copy(spread_r[:, :, :], spread[:, :, :])
                v.tensor_copy(first_row_r[:, :], first_row[:, :])
                v.tensor_copy(bo_hi[:, :], bo_row[:, :]).then_inc(dve_set, 1)
                dve.wait_ge(dve_set, 2)
                v.tensor_tensor(out=bo_lo[:, :], in0=bo_row[:, :], in1=bo_hi[:, :].bitcast(F32),
                                op=ALU.subtract).then_inc(dve_set, 1)

            run(DVE_ORDER, {
                "products": products, "max and shift": shift_scores, "sum of v": value_total,
                "inverse": inverse, "rests": low_parts, "weights * v": weighted_values,
                "spikes": count_spikes,
                "moments in": in_moments, "moments mid": mid_moments, "moments ff": ff_moments,
                "moments out": out_moments}, constants)

        @block.tensor
        def _(pe):
            t = nc.tensor

            def bank_for(stage, b, h, n):
                at = fill(stage, b, h) + n - NX + 1
                if at >= 1:
                    pe.wait_ge(x_emptied, at)
                return (fill_bank(stage, b, h) + n) % NX

            def turn(stage, norm, b, h, src):
                pe.wait_ge(ln_done[norm], 2 * b + h + 1)
                bank = xbank[bank_for(stage, b, h, 0)]
                for i in range(4):
                    last = t.transpose(bank[:, i * P:(i + 1) * P], src[:, 4 * h + i, :], ident[:, :])
                last.then_inc(x_filled, 1)

            def project(stage, w, b):
                if first(b):
                    pe.wait_ge(early_in, 16 * len(EARLY))
                pe.wait_ge(x_emptied, fill("turn in", b, 1) + 1)
                for n in range(2):
                    bank = xbank[bank_for(stage, b, 0, n)]
                    t.matmul(bank[:, :], w[:, :], xnT_in[:, n * HALF:(n + 1) * HALF], start=True,
                             stop=True).then_inc(x_filled, 1)

            def score(b, g):
                pe.wait_ge(qk_ready, NG * b + g + 1)
                if first(b):
                    pe.wait_ge(pool_set, 4)
                    pe.wait_ge(dve_set, 1)
                if not first(b) and g == 0:
                    pe.wait_ge(shifted, b)
                k0, k1 = GROUPS[g][0], GROUPS[g][-1] + 1
                for half in range(2):
                    for j in range(4):
                        tok = (2 * j + half) * P
                        last = t.matmul(scores[32 * j:32 * j + 32, k0:k1, :], head_sum[:, half, :],
                                        qk[:, k0:k1, tok:tok + P], start=half == 0, stop=half == 1)
                last.then_inc(scores_ready, 1)

            def spread_weights(b, h):
                pe.wait_ge(hi_ready, 2 * b + h + 1)
                pe.wait_ge(lo_ready[h], b + 1)
                if first(b):
                    pe.wait_ge(dve_set, 2)
                for i, (slots, t0, blocks) in enumerate(SPREADS[h]):
                    n = S0 * h + i
                    if not first(b) or n >= NW:
                        pe.wait_ge(wv_ready, NS * b + n - NW + 1)
                    ks = slice(slots[0], slots[-1] + 1)
                    bank = wbank[n % NW][:, 0:len(slots) * blocks * P]\
                        .rearrange("p (k t) -> p k t", k=len(slots))
                    for i in range(blocks):
                        last = t.matmul(bank[:, :, i * P:(i + 1) * P],
                                        spread_r[:, (t0 + i) % (TB // 2), :],
                                        wt_parts[:, h, ks, :], start=True, stop=True)
                    last.then_inc(spread_ready, 1)

            def attention_out(b, h):
                bank = bank_for("attention", b, h, 0)
                if first(b):
                    pe.wait_ge(dve_set, 3)
                for part, start in ((bo_hi, True), (bo_lo, False)):
                    t.matmul(rows_of(bank), first_row_r[:, :],
                             part[:, :].unsqueeze(1).to_broadcast([P, 4, D]), start=start, stop=False)
                pe.wait_ge(merged, NM * (2 * b + h + 1))
                pe.wait_ge(wv_ready, NS * b + (NS if h else S0))
                for i in range(4):
                    tok = (4 * h + i) * P
                    for k in (0, 1, NK - 1):
                        last = t.matmul(xbank[bank][:, i * P:(i + 1) * P], wv[:, k, tok:tok + P],
                                        wo_sb[:, :], start=False, stop=i == 3 and k == NK - 1)
                last.then_inc(x_filled, 1)

            def feed_forward_up(b, h):
                if first(b):
                    pe.wait_ge(late_in, 32)
                pe.wait_ge(x_emptied, fill("turn ff", b, h) + 1)
                for f in range(FB):
                    bank = xbank[bank_for("up", b, h, f)]
                    t.matmul(bank[:, :], wfc_sb[:, f * P:(f + 1) * P],
                             xnT_ff[:, h * HALF:(h + 1) * HALF], start=True, stop=True)\
                        .then_inc(x_filled, 1)

            def feed_forward_down(b, h):
                bank = xbank[bank_for("down", b, h, 0)]
                pe.wait_ge(hid_ready, FB * (2 * b + h + 1))
                for i in range(4):
                    tok = (4 * h + i) * P
                    for f in range(FB):
                        last = t.matmul(bank[:, i * P:(i + 1) * P], hid[:, f, tok:tok + P],
                                        wproj_sb[:, f, :], start=f == 0, stop=f == FB - 1)
                last.then_inc(x_filled, 1)

            pe.wait_ge(pool_set, 3)
            run(PE_ORDER, {
                "values": lambda b, h: project("values", wv_sb, b),
                "queries": lambda b, h: project("queries", wq_sb, b),
                "keys": lambda b, h: project("keys", wk_sb, b),
                "turn in": lambda b, h: turn("turn in", "in", b, h, xn_in),
                "turn ff": lambda b, h: turn("turn ff", "ff", b, h, xn_ff),
                "scores": score, "spread": spread_weights, "attention": attention_out,
                "up": feed_forward_up, "down": feed_forward_down})


def kernel(L0_attn_x, L0_attn_Wq, L0_attn_bq, L0_attn_Wk, L0_attn_bk, L0_attn_Wv, L0_attn_bv,
           L0_attn_Wo, L0_attn_bo, L0_ffn_W_fc, L0_ffn_W_proj):
    import concourse.bacc as bacc
    from concourse.bass_utils import run_bass_kernel_spmd

    col = lambda a: np.asarray(a).reshape(-1, 1)
    laid = {
        "x": np.asarray(L0_attn_x),
        "wq_t": np.asarray(L0_attn_Wq).T, "bq": col(L0_attn_bq),
        "wk_t": np.asarray(L0_attn_Wk).T, "bk": col(L0_attn_bk),
        "wv_t": np.asarray(L0_attn_Wv).T, "bv": col(L0_attn_bv),
        "wo_t": np.asarray(L0_attn_Wo).T, "bo": np.asarray(L0_attn_bo).reshape(1, -1),
        "wfc_t": np.asarray(L0_ffn_W_fc).T, "wproj_t": np.asarray(L0_ffn_W_proj).T,
    }
    laid = {n: np.ascontiguousarray(a) for n, a in laid.items()}
    nc = bacc.Bacc("TRN2", target_bir_lowering=False, num_devices=1)
    args = [nc.dram_tensor(n, a.shape, F32, kind="ExternalInput").ap() for n, a in laid.items()]
    out = nc.dram_tensor("out", laid["x"].shape, F32, kind="ExternalOutput").ap()
    log_sparse_block(nc, *args, out)
    result = run_bass_kernel_spmd(nc, [laid], core_ids=[0])
    return result.results[0]["out"]
```
